# Optimizing a Trainium2 kernel written in Bass

```python
import numpy as np
import jax
import jax.numpy as jnp

def _softmax(x, axis=-1):
    return jax.nn.softmax(x, axis=axis)
def _gelu(x):
    return jax.nn.gelu(x, approximate=True)
def _silu(x):
    return jax.nn.silu(x)
def _sigmoid(x):
    return jax.nn.sigmoid(x)
def _layernorm(x, axis=-1, eps=1e-5):
    m = jnp.mean(x, axis=axis, keepdims=True)
    v = jnp.var(x, axis=axis, keepdims=True)
    return (x - m) / jnp.sqrt(v + eps)
def _scatter_add(tgt, idx, src, axis=0):
    return tgt.at[idx].add(src)
def _segment_sum(src, seg, n):
    return jax.ops.segment_sum(src, seg, n)

kernel_name = 'mk_rec_standalone_d1_rec_7aafb6'

def setup_inputs(seed: int = 0):
    np.random.seed(seed)
    _w = jnp.asarray
    def _rec_inputs():
        import jax
        import jax.numpy as jnp
        _rk = jax.random.key(seed)
        r_x = -0.000153849 + 1.00027 * jax.random.normal(jax.random.fold_in(_rk, 1), (4096, 24, 128), jnp.float32)
        return r_x
    r_x = _rec_inputs()
    def _L0_rec_setup():
        import jax, jax.numpy as jnp
        import numpy as np
        import itertools
        key = jax.random.key(seed)
        k1, k2 = jax.random.split(key)
        B, F, E = (2048, 24, 128)
        P = F * (F - 1) // 2
        x = jax.random.normal(k1, (B, F, E), dtype=jnp.float32)
        W = jax.random.normal(k2, (P, E, E), dtype=jnp.float32) * (1.0 / np.sqrt(E))
        return {'x': x, 'W': W}
    _L0_rec_all = _L0_rec_setup()
    _L0_rec_in = {k: v for k, v in _L0_rec_all.items() if k in ('W', )}
    del _L0_rec_all

    return {
        "r_x": r_x,
        "L0_rec_W": _L0_rec_in["W"],
    }

def reference(r_x, L0_rec_W):
    import jax
    import jax.numpy as jnp
    def _L0_rec_ref(x, W):
        import jax, jax.numpy as jnp
        import numpy as np
        import itertools
        F = x.shape[1]
        pairs = np.array(list(itertools.combinations(range(F), 2)), dtype=np.int32)
        pi, pj = (pairs[:, 0], pairs[:, 1])
        xi = x[:, pi, :]
        xj = x[:, pj, :]
        p = jnp.einsum('bpe,pef->bpf', xi, W) * xj
        return p

    y = _L0_rec_ref(r_x, L0_rec_W)
    return y


_drawn_inputs = setup_inputs


def setup_inputs(seed=0):
    import zlib

    import numpy as np

    out = dict(_drawn_inputs(seed))
    spreads = {}
    factors = {}
    for name, (base, spread) in spreads.items():
        noise = np.random.default_rng([zlib.crc32(name.encode()), seed]).standard_normal(out[name].shape)
        drawn = base * np.exp(spread * noise) if base else spread * noise
        out[name] = jnp.asarray(drawn.astype(out[name].dtype))
    for name, factor in factors.items():
        out[name] = (out[name] * factor).astype(out[name].dtype)
    return out
```

```python
from contextlib import ExitStack

import concourse.bass as bass
import concourse.mybir as mybir
from concourse.alu_op_type import AluOpType

F32 = mybir.dt.float32
ACT = mybir.ActivationFunctionType

P = 128
BANK = 512
UNROLL = 2
RING = 6
SEG_BANKS = 2
SLOT_PAIRS = 13
SLOTS = 5


class Plan:

    def __init__(self, fields, emb):
        per_bank = BANK // emb
        self.banks = []
        self.segments = []
        pair = 0
        for i in range(fields - 1):
            left = fields - 1 - i
            while left:
                at = len(self.banks) % RING
                n = min(left, per_bank * min(SEG_BANKS, RING - at))
                for m in range(0, n, per_bank):
                    self.banks.append((i, pair + m, min(per_bank, n - m), at + m // per_bank))
                self.segments.append((i, pair, n, at, len(self.banks)))
                pair += n
                left -= n
        assert len(self.banks) % RING == 0
        self.first_pair = [i * (2 * fields - i - 1) // 2 for i in range(fields)]
        self.parcels = []
        for s, (_, first, n, _, _) in enumerate(self.segments):
            if self.parcels and first + n - self.parcels[-1][0] <= SLOT_PAIRS:
                self.parcels[-1][1] += n
                self.parcels[-1][3] = s + 1
            else:
                self.parcels.append([first, n, s, s + 1])
        self.batches = [list(range(f, min(f + per_bank, fields - 1))) for f in range(0, fields - 1, per_bank)]
        self.pairs = pair


def pair_products(nc, x, w, out):
    rows, fields, emb = x.shape
    plan = Plan(fields, emb)
    per_bank = BANK // emb
    tiles = rows // P
    rounds = tiles // UNROLL
    n_banks, n_segs, n_parcels, n_batches = (
        len(plan.banks), len(plan.segments), len(plan.parcels), len(plan.batches))
    assert (UNROLL * n_parcels) % SLOTS == 0 and tiles % UNROLL == 0 and rounds >= 3
    batch_after = {plan.batches[b][-1] + 1: b for b in range(n_batches - 1)}
    late_after = 2
    late = n_batches - 1
    slot_uses = UNROLL * n_parcels // SLOTS

    x_v = x.rearrange("(t p) f e -> t p (f e)", p=P)
    out_v = out.rearrange("(t p) q e -> t p (q e)", p=P)
    w_v = w.rearrange("q e f -> e q f")

    ctx = ExitStack()
    with ctx:
        def sb(name, shape):
            return ctx.enter_context(nc.sbuf_tensor(name, shape, F32))

        w_sb = sb("w_sb", [P, plan.pairs, emb])
        x_sb = [sb(f"x_sb{u}", [P, fields * emb]) for u in range(UNROLL)]
        xt_sb = sb("xt_sb", [P, (fields - 1) * P])
        stage = [sb(f"stage{s}", [P, SLOT_PAIRS * emb]) for s in range(SLOTS)]
        ident = sb("ident", [P, P])
        products = ctx.enter_context(nc.psum_tensor("products", [P, RING * BANK], F32))
        turned = [ctx.enter_context(nc.psum_tensor(f"turned{k}", [P, BANK], F32)) for k in range(2)]

        sem = lambda name: ctx.enter_context(nc.semaphore(name))
        ident_zeroed = sem("ident_zeroed")
        ident_ready = sem("ident_ready")
        x_loaded = [sem(f"x_loaded{u}") for u in range(UNROLL)]
        w_loaded = [sem(f"w_loaded{i}") for i in range(fields - 1)]
        turned_ready = sem("turned_ready")
        xt_ready = sem("xt_ready")
        products_ready = sem("products_ready")
        multiplied = sem("multiplied")
        stored = [sem(f"stored{s}") for s in range(SLOTS)]

        block = ctx.enter_context(nc.Block())

        def for_all_rounds(eng, body):
            body(0, True, False)
            with eng.Fori(1, rounds - 1) as g:
                body(g, False, False)
            body(rounds - 1, False, True)

        def at_least(eng, semaphore, per_round, g, rest):
            if isinstance(g, int) and per_round * g + rest <= 0:
                return
            eng.wait_ge(semaphore, g * per_round + rest)

        @block.sync
        def _(sp):
            def load_x(g, u):
                sp.dma_start(x_sb[u][:, :], x_v[g * UNROLL + u]).then_inc(x_loaded[u], 16)

            def round_(g, first, last):
                for u in range(UNROLL):
                    if not (last and u == UNROLL - 1):
                        if u == 0:
                            at_least(sp, multiplied, UNROLL * n_segs, g, 0)
                            load_x(g, 1)
                        else:
                            at_least(sp, multiplied, UNROLL * n_segs, g, n_segs)
                            load_x(g + 1, 0)
                    for k, (pair, n, _, end) in enumerate(plan.parcels):
                        slot = (u * n_parcels + k) % SLOTS
                        at_least(sp, multiplied, UNROLL * n_segs, g, u * n_segs + end)
                        sp.dma_start(out_v[g * UNROLL + u, :, pair * emb:(pair + n) * emb],
                                     stage[slot][:, 0:n * emb]).then_inc(stored[slot], 16)

            sp.dma_start(x_sb[0][:, :], x_v[0]).then_inc(x_loaded[0], 16)
            for_all_rounds(sp, round_)
            for s in range(SLOTS):
                sp.wait_ge(stored[s], 16 * rounds * slot_uses)

        @block.gpsimd
        def _(pool):
            nc.gpsimd.memset(ident[:, :], 0.0).then_inc(ident_zeroed, 1)
            pool.wait_ge(ident_zeroed, 1)
            nc.gpsimd.affine_select(out=ident[:, :], in_=ident[:, :], compare_op=AluOpType.not_equal, fill=1.0,
                                    base=0, pattern=[[-1, P]], channel_multiplier=1).then_inc(ident_ready, 1)

        @block.scalar
        def _(act):
            for i in range(fields - 1):
                a, b = plan.first_pair[i], plan.first_pair[i + 1]
                act.dma_start(w_sb[:, a:b, :], w_v[:, a:b, :]).then_inc(w_loaded[i], 16)

            def copy_batch(g, u, b):
                n = u * n_batches + b
                at_least(act, turned_ready, UNROLL * n_batches, g, n + 1)
                a = plan.batches[b][0]
                cols = len(plan.batches[b]) * P
                nc.scalar.activation(xt_sb[:, a * P:a * P + cols], turned[n % 2][:, 0:cols],
                                     ACT.Copy).then_inc(xt_ready, 1)

            def round_(g, first, last):
                for u in range(UNROLL):
                    copy_batch(g, u, late)
                    if not (last and u == UNROLL - 1):
                        for b in range(n_batches - 1):
                            copy_batch(g + u // (UNROLL - 1), (u + 1) % UNROLL, b)

            for b in range(n_batches - 1):
                copy_batch(0, 0, b)
            for_all_rounds(act, round_)

        @block.vector
        def _(dve):
            def round_(g, first, last):
                for u in range(UNROLL):
                    at_least(dve, x_loaded[u], 16, g, 16)
                    for k, (pair0, _, start, end) in enumerate(plan.parcels):
                        use = u * n_parcels + k
                        slot = use % SLOTS
                        at_least(dve, stored[slot], 16 * slot_uses, g, 16 * (use // SLOTS))
                        for i, pair, n, bank, filled in plan.segments[start:end]:
                            at_least(dve, products_ready, UNROLL * n_banks, g, u * n_banks + filled)
                            j = i + 1 + pair - plan.first_pair[i]
                            nc.vector.tensor_tensor(
                                stage[slot][:, (pair - pair0) * emb:(pair - pair0 + n) * emb],
                                products[:, bank * BANK:bank * BANK + n * emb],
                                x_sb[u][:, j * emb:(j + n) * emb], AluOpType.mult).then_inc(multiplied, 1)

            for_all_rounds(dve, round_)

        @block.tensor
        def _(pe):
            freed_by = {c: next(s + 1 for s, seg in enumerate(plan.segments) if seg[4] > c)
                        for c in range(n_banks)}

            def turn_batch(g, u, b):
                n = u * n_batches + b
                if b == 0:
                    at_least(pe, x_loaded[u], 16, g, 16)
                at_least(pe, xt_ready, UNROLL * n_batches, g, n - 1)
                for k, f in enumerate(plan.batches[b]):
                    last_turn = nc.tensor.transpose(turned[n % 2][:, k * P:(k + 1) * P],
                                                    x_sb[u][:, f * emb:(f + 1) * emb], ident[:, :])
                last_turn.then_inc(turned_ready, 1)

            def tile_(g, u, first, last):
                waited = None
                for c, (i, pair, n, bank) in enumerate(plan.banks):
                    new_field = c == 0 or plan.banks[c - 1][0] != i
                    if new_field:
                        if i - 1 in batch_after and not (last and u == UNROLL - 1):
                            turn_batch(g + u // (UNROLL - 1), (u + 1) % UNROLL, batch_after[i - 1])
                        if i == late_after + 1:
                            turn_batch(g, u, late)
                        if i % per_bank == 0:
                            b = i // per_bank
                            at_least(pe, xt_ready, UNROLL * n_batches, g, u * n_batches + b + 1)
                        if first and u == 0:
                            pe.wait_ge(w_loaded[i], 16)
                    back = c - RING
                    need = freed_by[back] if back >= 0 else freed_by[back + n_banks] - n_segs
                    if need != waited:
                        at_least(pe, multiplied, UNROLL * n_segs, g, u * n_segs + need)
                        waited = need
                    nc.tensor.matmul(products[:, bank * BANK:bank * BANK + n * emb],
                                     xt_sb[:, i * P:(i + 1) * P], w_sb[:, pair:pair + n, :],
                                     start=True, stop=True).then_inc(products_ready, 1)

            def round_(g, first, last):
                for u in range(UNROLL):
                    tile_(g, u, first, last)

            pe.wait_ge(ident_ready, 1)
            for b in range(n_batches - 1):
                turn_batch(0, 0, b)
            for_all_rounds(pe, round_)


def kernel(r_x, L0_rec_W):
    import numpy as np
    import concourse.bacc as bacc
    from concourse import mybir
    from concourse.bass_utils import run_bass_kernel_spmd

    x = np.ascontiguousarray(r_x)
    w = np.ascontiguousarray(L0_rec_W)
    rows, fields, emb = x.shape
    nc = bacc.Bacc("TRN2", target_bir_lowering=False, num_devices=1)
    x_d = nc.dram_tensor("x_dram", x.shape, mybir.dt.float32, kind="ExternalInput").ap()
    w_d = nc.dram_tensor("w_dram", w.shape, mybir.dt.float32, kind="ExternalInput").ap()
    out_d = nc.dram_tensor("out_dram", (rows, w.shape[0], emb), mybir.dt.float32, kind="ExternalOutput").ap()
    pair_products(nc, x_d, w_d, out_d)
    r = run_bass_kernel_spmd(nc, [{"x_dram": x, "w_dram": w}], core_ids=[0])
    return r.results[0]["out_dram"]
```
